# Optimizing a Trainium2 kernel written in Bass

```python
import numpy as np
import jax
import jax.numpy as jnp

def _softmax(x, axis=-1):
    return jax.nn.softmax(x, axis=axis)

def _gelu(x):
    return jax.nn.gelu(x, approximate=True)

def _silu(x):
    return jax.nn.silu(x)

def _sigmoid(x):
    return jax.nn.sigmoid(x)

def _layernorm(x, axis=-1, eps=1e-05):
    m = jnp.mean(x, axis=axis, keepdims=True)
    v = jnp.var(x, axis=axis, keepdims=True)
    return (x - m) / jnp.sqrt(v + eps)

def _scatter_add(tgt, idx, src, axis=0):
    return tgt.at[idx].add(src)

def _segment_sum(src, seg, n):
    return jax.ops.segment_sum(src, seg, n)
kernel_name = 'mk_adj_resnorm_d1_adj_r2_e74a3f'

def setup_inputs(seed: int=0):
    np.random.seed(seed)
    _w = jnp.asarray

    def _rec_inputs():
        import jax
        import jax.numpy as jnp
        _gk = jax.random.key(seed)
        x = -0.000929 + 1 * jax.random.normal(jax.random.fold_in(_gk, 1), (8192, 64), jnp.float32)
        _w = (1.0 + jnp.arange(8192, dtype=jnp.float32)) ** (-0.5)
        _w = _w / _w.mean()
        _pij = jnp.clip(0.000488281 * _w[:, None] * _w[None, :], 0.0, 1.0)
        _a = jax.random.uniform(jax.random.fold_in(_gk, 2), (8192, 8192)) < _pij
        _a = jnp.logical_or(_a, jnp.eye(8192, dtype=bool))
        _af = _a.astype(jnp.float32)
        _af = _af * jax.random.uniform(jax.random.fold_in(_gk, 3), (8192, 8192), jnp.float32, 0.05, 1)
        adj = _af
        return (x, adj)
    x, adj = _rec_inputs()

    def _L0_gnn_setup():
        import jax, jax.numpy as jnp
        import numpy as np
        P_DROP = 0.1
        key = jax.random.key(seed)
        k1, k2, k3 = jax.random.split(key, 3)
        N, D = (8192, 64)
        x = jax.random.normal(k1, (N, D), dtype=jnp.float32)
        adj = jax.random.uniform(k2, (N, N), dtype=jnp.float32)
        u = jax.random.uniform(k3, (N, D), dtype=jnp.float32)
        return {'x': x, 'adj': adj, 'u': u}
    _L0_gnn_all = _L0_gnn_setup()
    _L0_gnn_in = {k: v for k, v in _L0_gnn_all.items() if k in ('u',)}
    del _L0_gnn_all
    return {'x': x, 'adj': adj, 'L0_gnn_u': _L0_gnn_in['u']}

def reference(x, adj, L0_gnn_u):
    import jax
    import jax.numpy as jnp

    def _L0_gnn_ref(x, adj, u):
        import jax, jax.numpy as jnp
        import numpy as np
        P_DROP = 0.1
        keep = (u >= P_DROP).astype(x.dtype)
        x_drop = x * keep / (1.0 - P_DROP)
        return jnp.matmul(adj, x_drop)
    x = _layernorm(x + _L0_gnn_ref(x, adj, L0_gnn_u), axis=-1)
    return x

_drawn_inputs = setup_inputs


def setup_inputs(seed=0):
    import zlib

    import numpy as np

    out = dict(_drawn_inputs(seed))
    spreads = {}
    factors = {}
    for name, (base, spread) in spreads.items():
        noise = np.random.default_rng([zlib.crc32(name.encode()), seed]).standard_normal(out[name].shape)
        drawn = base * np.exp(spread * noise) if base else spread * noise
        out[name] = jnp.asarray(drawn.astype(out[name].dtype))
    for name, factor in factors.items():
        out[name] = (out[name] * factor).astype(out[name].dtype)
    return out
```

```python
from contextlib import ExitStack

import concourse.bass as bass
from concourse import mybir

F32 = mybir.dt.float32
ALU = mybir.AluOpType

P = 128
Q = 4
B = 32
P_DROP = 0.1
EPS = 1e-5


def build(nc, x, adj, u, out):
    N, D = x.shape
    ROWS = 512
    G = N // ROWS
    KQ = N // Q
    KC = 512
    C = KQ // KC
    J = KC // B
    TH = ROWS // B // 2
    UNITS = 2 * C
    RING = 4
    W = ROWS // P
    LOADED = 16 * Q
    assert G % 2 == 0 and UNITS % RING == 0 and C % 2 == 0 and 2 * D == P

    adj_v = adj.rearrange("(g t r) (q k) -> g q r t k", g=G, r=B, q=Q)
    x_v = x.rearrange("(q k s) d -> q s k d", q=Q, s=B)
    u_v = u.rearrange("(q k s) d -> q s k d", q=Q, s=B)
    x_rows = x.rearrange("(g p w) d -> g p (w d)", g=G, w=W)
    out_rows = out.rearrange("(g p w) d -> g p (w d)", g=G, w=W)

    with ExitStack() as ctx:
        def sb(name, shape):
            return ctx.enter_context(nc.sbuf_tensor(name, shape, F32))

        def psum(name, shape):
            return ctx.enter_context(nc.psum_tensor(name, shape, F32))

        def sem(name):
            return ctx.enter_context(nc.semaphore(name))

        adj_in = sb("adj_in", [P, RING, TH * KC])
        adj_t = sb("adj_t", [P, 2, J * ROWS])
        x_drop = sb("x_drop", [P, C * J, D])
        u_sb = sb("u_sb", [P, C * J, D])
        fold = sb("fold", [P, D])
        sums = sb("sums", [P, ROWS])
        x_res = sb("x_res", [P, 2, W * D])
        h = sb("h", [P, 2, W * D])
        stats = sb("stats", [P, W, 6])
        mean_var = sb("mean_var", [P, 2, W, 2])
        var_eps = sb("var_eps", [P, 2, W])
        neg_half = sb("neg_half", [P, W])
        rstd = sb("rstd", [P, W])
        y = sb("y", [P, 2, W * D])
        acc = [psum(f"acc{i}", [P, 512]) for i in range(2)]
        agg = psum("agg", [P, 512])

        adj_loaded = [sem(f"adj_loaded{i}") for i in range(RING)]
        x_loaded = sem("x_loaded")
        x_dropped = sem("x_dropped")
        unit_turned = sem("unit_turned")
        chunk_used = sem("chunk_used")
        sums_copied = sem("sums_copied")
        agg_ready = sem("agg_ready")
        res_loaded = [sem(f"res_loaded{i}") for i in range(2)]
        h_ready = sem("h_ready")
        stats_ready = sem("stats_ready")
        stats_aggregated = sem("stats_aggregated")
        var_ready = sem("var_ready")
        rstd_ready = sem("rstd_ready")
        centred = sem("centred")
        h_free = sem("h_free")
        out_stored = [sem(f"out_stored{i}") for i in range(2)]
        fold_step = sem("fold_step")
        const_ready = sem("const_ready")

        def load_units(eng, quads, g, units, first):
            for n in units:
                if not first or n >= RING:
                    eng.wait_ge(unit_turned, g * UNITS + n - RING + 1)
                c, half = n // 2, n % 2
                for q in quads:
                    dst = adj_in[q * B:(q + 1) * B, n % RING, :].rearrange("p (t k) -> p t k", t=TH)
                    src = adj_v[g, q, :, half * TH:(half + 1) * TH, c * KC:(c + 1) * KC]
                    eng.dma_start(dst, src).then_inc(adj_loaded[n % RING], 16)

        def load_stream(eng, quads):
            load_units(eng, quads, 0, range(2), True)
            for q in quads:
                eng.dma_start(x_drop[q * B:(q + 1) * B, :, :], x_v[q]).then_inc(x_loaded, 16)
                eng.dma_start(u_sb[q * B:(q + 1) * B, :, :], u_v[q]).then_inc(x_loaded, 16)
            load_units(eng, quads, 0, range(2, UNITS), True)
            with eng.Fori(1, G) as g:
                load_units(eng, quads, g, range(UNITS), False)

        block = ctx.enter_context(nc.Block())

        @block.sync
        def _(sp):
            load_stream(sp, (0, 1))

        @block.scalar
        def _(act):
            load_stream(act, (2, 3))

        @block.vector
        def _(dve):
            def turn_units(g, units, first):
                for n in units:
                    c, half = n // 2, n % 2
                    dve.wait_ge(adj_loaded[n % RING], (g * (UNITS // RING) + n // RING + 1) * LOADED)
                    if half == 0 and (not first or c >= 2):
                        dve.wait_ge(chunk_used, g * C + c - 1)
                    src = adj_in[:, n % RING, :].rearrange("p (t j r) -> p t j r", t=TH, j=J)
                    dst = adj_t[:, c % 2, :].rearrange("p (j t r) -> p t j r", j=J, r=B)
                    nc.vector.transpose(dst[:, half * TH:(half + 1) * TH], src).then_inc(unit_turned, 1)

            def copy_sums(g, b):
                dve.wait_ge(chunk_used, (g + 1) * C)
                nc.vector.tensor_copy(sums[:, :], acc[b][:, :]).then_inc(sums_copied, 1)

            def add_residual(g, b):
                dve.wait_ge(agg_ready, g + 1)
                dve.wait_ge(res_loaded[b], (g - b) * 8 + 16)
                dve.wait_ge(h_free, g + 1)
                nc.vector.scalar_tensor_tensor(out=h[:, b, :], in0=agg[:, 0:W * D], scalar=1.0 / (1.0 - P_DROP),
                                               in1=x_res[:, b, :], op0=ALU.mult, op1=ALU.add).then_inc(h_ready, 1)

            def row_stats(b):
                for w in range(W):
                    nc.vector.bn_stats(out=stats[:, w, :], in_=h[:, b, w * D:(w + 1) * D]).then_inc(stats_ready, 1)

            def aggregate_stats(b):
                for w in range(W):
                    nc.vector.bn_aggr(out=mean_var[:, b, w, :], in_=stats[:, w, :]).then_inc(stats_aggregated, 1)

            def add_eps(b):
                nc.vector.tensor_scalar(var_eps[:, b, :], mean_var[:, b, :, 1], EPS, None, ALU.add).then_inc(var_ready, 1)

            def group(g, b):
                turn_units(g, range(0, 2), False)
                copy_sums(g - 1, 1 - b)
                turn_units(g, range(2, 4), False)
                add_residual(g - 1, 1 - b)
                dve.wait_ge(h_ready, g)
                turn_units(g, range(4, 5), False)
                row_stats(1 - b)
                dve.wait_ge(stats_ready, g * W)
                turn_units(g, range(5, 6), False)
                aggregate_stats(1 - b)
                dve.wait_ge(stats_aggregated, g * W)
                turn_units(g, range(6, 7), False)
                add_eps(1 - b)
                turn_units(g, range(7, UNITS), False)

            turn_units(0, range(2), True)
            dve.wait_ge(x_loaded, 2 * Q * 16)
            for c in range(C):
                steps = slice(c * J, (c + 1) * J)
                nc.vector.scalar_tensor_tensor(out=x_drop[:, steps, :], in0=u_sb[:, steps, :], scalar=P_DROP,
                                               in1=x_drop[:, steps, :], op0=ALU.is_ge,
                                               op1=ALU.mult).then_inc(x_dropped, 1)
            turn_units(0, range(2, UNITS), True)
            group(1, 1)
            with dve.Fori(1, G // 2) as pair:
                group(2 * pair, 0)
                group(2 * pair + 1, 1)
            copy_sums(G - 1, 1)
            add_residual(G - 1, 1)
            dve.wait_ge(h_ready, G)
            row_stats(1)
            dve.wait_ge(stats_ready, G * W)
            aggregate_stats(1)
            dve.wait_ge(stats_aggregated, G * W)
            add_eps(1)

        @block.tensor
        def _(pe):
            def contract(g, b, chunks, first=False, bank_used=True):
                for c in chunks:
                    pe.wait_ge(unit_turned, g * UNITS + 2 * c + 2)
                    if first:
                        pe.wait_ge(x_dropped, c + 1)
                    if c == 0 and bank_used:
                        pe.wait_ge(sums_copied, g - 1)
                    for j in range(J):
                        half = j % 2
                        last = nc.tensor.matmul(acc[b][half * D:(half + 1) * D, :], x_drop[:, c * J + j, :],
                                                adj_t[:, c % 2, j * ROWS:(j + 1) * ROWS],
                                                start=(c == 0 and j < 2), stop=(c == C - 1 and j >= J - 2))
                    last.then_inc(chunk_used, 1)

            def fold_halves(g):
                pe.wait_ge(sums_copied, g + 1)
                for w in range(W):
                    last = nc.tensor.matmul(agg[:, w * D:(w + 1) * D],
                                            sums[:, :].rearrange("k (p w) -> k w p", w=W)[:, w, :], fold[:, :],
                                            start=True, stop=True)
                last.then_inc(agg_ready, 1)

            def group(g, b):
                contract(g, b, range(0, 1))
                fold_halves(g - 1)
                contract(g, b, range(1, C))

            contract(0, 0, range(C), first=True, bank_used=False)
            contract(1, 1, range(0, 1), bank_used=False)
            pe.wait_ge(const_ready, 1)
            fold_halves(0)
            contract(1, 1, range(1, C))
            with pe.Fori(1, G // 2) as pair:
                group(2 * pair, 0)
                group(2 * pair + 1, 1)
            fold_halves(G - 1)

        @block.gpsimd
        def _(pool):
            def load_residual(g, b, first):
                if not first:
                    pool.wait_ge(h_ready, g - 1)
                pool.dma_start(x_res[:, b, :], x_rows[g]).then_inc(res_loaded[b], 16)

            def normalise(g, b, first):
                pool.wait_ge(var_ready, g + 1)
                nc.gpsimd.tensor_tensor(rstd[:, :], var_eps[:, b, :], neg_half[:, :], ALU.pow).then_inc(rstd_ready, 1)
                if not first:
                    pool.wait_ge(out_stored[b], (g - b) * 8)
                y_rows = y[:, b, :].rearrange("p (w d) -> p w d", w=W)
                nc.gpsimd.tensor_tensor(y_rows, h[:, b, :].rearrange("p (w d) -> p w d", w=W),
                                        mean_var[:, b, :, 0:1].broadcast_to([P, W, D]),
                                        ALU.subtract).then_inc(centred, 1)
                pool.wait_ge(rstd_ready, g + 1)
                pool.wait_ge(centred, g + 1)
                last = nc.gpsimd.tensor_tensor(y_rows, y_rows, rstd[:, :].rearrange("p (w d) -> p w d", d=1).broadcast_to([P, W, D]),
                                               ALU.mult)
                last.then_inc(h_free, 1)
                pool.wait_ge(h_free, g + 3)
                pool.dma_start(out_rows[g], y[:, b, :]).then_inc(out_stored[b], 16)

            pool.sem_inc(h_free, 2)
            load_residual(0, 0, True)
            load_residual(1, 1, True)
            nc.gpsimd.memset(fold[:, :], 0.0).then_inc(fold_step, 1)
            nc.gpsimd.memset(neg_half[:, :], -0.5).then_inc(fold_step, 1)
            pool.wait_ge(fold_step, 2)
            nc.gpsimd.affine_select(out=fold[:, :], in_=fold[:, :], compare_op=ALU.not_equal, fill=1.0, base=0,
                                    pattern=[[-1, D]], channel_multiplier=1).then_inc(fold_step, 1)
            pool.wait_ge(fold_step, 3)
            nc.gpsimd.affine_select(out=fold[:, :], in_=fold[:, :], compare_op=ALU.not_equal, fill=1.0, base=-D,
                                    pattern=[[-1, D]], channel_multiplier=1).then_inc(const_ready, 1)
            for b in range(2):
                normalise(b, b, True)
                load_residual(b + 2, b, False)
            with pool.Fori(1, G // 2 - 1) as pair:
                for b in range(2):
                    normalise(2 * pair + b, b, False)
                    load_residual(2 * pair + b + 2, b, False)
            for b in range(2):
                normalise(G - 2 + b, b, False)
            for b in range(2):
                pool.wait_ge(out_stored[b], G // 2 * 16)


def kernel(x, adj, L0_gnn_u):
    import numpy as np
    import concourse.bacc as bacc
    from concourse.bass_utils import run_bass_kernel_spmd

    nc = bacc.Bacc("TRN2", target_bir_lowering=False, num_devices=1)
    arrays, args = {}, []
    for name, a in (("x", x), ("adj", adj), ("u", L0_gnn_u)):
        a = np.ascontiguousarray(a)
        arrays[name] = a
        args.append(nc.dram_tensor(name, a.shape, mybir.dt.from_np(a.dtype), kind="ExternalInput").ap())
    out = nc.dram_tensor("out", x.shape, F32, kind="ExternalOutput").ap()
    build(nc, *args, out)
    r = run_bass_kernel_spmd(nc, [arrays], core_ids=[0])
    return r.results[0]["out"]
```

```python
from contextlib import ExitStack

import concourse.bass as bass
from concourse import mybir

F32 = mybir.dt.float32
ALU = mybir.AluOpType

P = 128
Q = 4
B = 32
P_DROP = 0.1
EPS = 1e-5


def build(nc, x, adj, u, out):
    N, D = x.shape
    G = 16
    ROWS = N // G
    RP = ROWS // Q
    TB = RP // B
    KQ = N // Q
    KC = 512
    C = KQ // KC
    J = KC // B
    E = 2
    UNITS = C * Q
    RING = 8
    W = ROWS // P
    LOADED = 16 * Q
    assert ROWS == 512 and G % 2 == 0 and UNITS % RING == 0 and C % 2 == 0 and 2 * D == P and W == TB

    adj_v = adj.rearrange("(a g t r) (q k) -> g a q r t k", a=Q, t=TB, r=B, q=Q)
    x_v = x.rearrange("(q k s e) d -> q s k (e d)", q=Q, s=B, e=E)
    u_v = u.rearrange("(q k s e) d -> q s k (e d)", q=Q, s=B, e=E)
    out_v = out.rearrange("(q k s e) d -> q s k (e d)", q=Q, s=B, e=E)
    STEPS = C * J

    with ExitStack() as ctx:
        def sb(name, shape):
            return ctx.enter_context(nc.sbuf_tensor(name, shape, F32))

        def psum(name, shape):
            return ctx.enter_context(nc.psum_tensor(name, shape, F32))

        def sem(name):
            return ctx.enter_context(nc.semaphore(name))

        adj_in = sb("adj_in", [P, RING, TB * KC])
        adj_t = sb("adj_t", [P, 2, J * ROWS])
        x_sb = sb("x_sb", [P, STEPS * D])
        x_drop = sb("x_drop", [P, STEPS * D])
        fold = sb("fold", [P, D])
        sums = sb("sums", [P, ROWS])
        h = sb("h", [P, 2, W * D])
        stats = sb("stats", [P, W, 6])
        mean_var = sb("mean_var", [P, 2, W, 2])
        var_eps = sb("var_eps", [P, 2, W])
        neg_half = sb("neg_half", [P, W])
        rstd = sb("rstd", [P, 2, W])
        y = sb("y", [P, 2, W * D])
        acc = [psum(f"acc{i}", [P, 512]) for i in range(2)]
        agg = psum("agg", [P, 512])

        adj_loaded = [sem(f"adj_loaded{i}") for i in range(RING)]
        x_loaded = sem("x_loaded")
        x_dropped = sem("x_dropped")
        unit_turned = sem("unit_turned")
        chunk_used = sem("chunk_used")
        sums_copied = sem("sums_copied")
        agg_ready = sem("agg_ready")
        h_ready = sem("h_ready")
        stats_ready = sem("stats_ready")
        stats_aggregated = sem("stats_aggregated")
        var_ready = sem("var_ready")
        rstd_ready = sem("rstd_ready")
        centred = sem("centred")
        h_free = sem("h_free")
        out_stored = sem("out_stored")
        last_centred = sem("last_centred")
        last_y_ready = sem("last_y_ready")
        last_stored = [sem(f"last_stored{i}") for i in range(2)]
        fold_step = sem("fold_step")
        const_ready = sem("const_ready")

        def load_units(eng, quads, g, units, ring_used):
            for n in units:
                if ring_used or n >= RING:
                    eng.wait_ge(unit_turned, g * UNITS + n - RING + 1)
                c, a = n // Q, n % Q
                for q in quads:
                    dst = adj_in[q * B:(q + 1) * B, n % RING, :].rearrange("p (t k) -> p t k", t=TB)
                    src = adj_v[g, a, q, :, :, c * KC:(c + 1) * KC]
                    eng.dma_start(dst, src).then_inc(adj_loaded[n % RING], 16)

        def load_stream(eng, quads):
            for q in quads:
                part = slice(q * B, (q + 1) * B)
                eng.dma_start(x_sb[part, :].rearrange("p (k f) -> p k f", f=E * D), x_v[q]).then_inc(x_loaded, 16)
                eng.dma_start(x_drop[part, :].rearrange("p (k f) -> p k f", f=E * D), u_v[q]).then_inc(x_loaded, 16)
            load_units(eng, quads, 0, range(UNITS), False)
            with eng.Fori(1, G) as g:
                load_units(eng, quads, g, range(UNITS), True)

        def store_last_group(eng, quads, stored):
            eng.wait_ge(last_y_ready, 1)
            for q in quads:
                eng.dma_start(out_v[q, :, (G - 1) * (W // E):G * (W // E), :],
                              y[q * B:(q + 1) * B, 1, :].rearrange("p (k f) -> p k f", f=E * D)).then_inc(stored, 16)
            eng.wait_ge(stored, 16 * len(quads))

        block = ctx.enter_context(nc.Block())

        @block.sync
        def _(sp):
            load_stream(sp, (0, 1))
            store_last_group(sp, (0, 1), last_stored[0])

        @block.scalar
        def _(act):
            load_stream(act, (2, 3))
            store_last_group(act, (2, 3), last_stored[1])

        @block.vector
        def _(dve):
            def turn_units(g, units, buffers_used=True):
                for n in units:
                    c, a = n // Q, n % Q
                    dve.wait_ge(adj_loaded[n % RING], (g * (UNITS // RING) + n // RING + 1) * LOADED)
                    if a == 0 and (buffers_used or c >= 2):
                        dve.wait_ge(chunk_used, g * C + c - 1)
                    src = adj_in[:, n % RING, :].rearrange("p (t k s e) -> p e t k s", t=TB, s=B, e=E)
                    dst = adj_t[:, c % 2, :].rearrange("p (k e a t r) -> p a e t k r", e=E, a=Q, t=TB, r=B)[:, a]
                    for e in range(E):
                        last = nc.vector.transpose(dst[:, e], src[:, e])
                    last.then_inc(unit_turned, 1)

            def copy_sums(g, b):
                dve.wait_ge(chunk_used, (g + 1) * C)
                src = acc[b][:, :].rearrange("f (q k s e) -> f e q k s", q=Q, s=B, e=E)
                dst = sums[:, :].rearrange("f (k e q s) -> f e q k s", q=Q, s=B, e=E)
                for e in range(E):
                    last = nc.vector.tensor_copy(dst[:, e], src[:, e])
                last.then_inc(sums_copied, 1)

            def add_residual(g, b):
                dve.wait_ge(agg_ready, g + 1)
                dve.wait_ge(h_free, g + 1)
                nc.vector.scalar_tensor_tensor(out=h[:, b, :], in0=agg[:, 0:W * D], scalar=1.0 / (1.0 - P_DROP),
                                               in1=x_sb[:, bass.ds(g * (W * D), W * D)], op0=ALU.mult,
                                               op1=ALU.add).then_inc(h_ready, 1)

            def row_stats(b):
                for w in range(W):
                    nc.vector.bn_stats(out=stats[:, w, :], in_=h[:, b, w * D:(w + 1) * D]).then_inc(stats_ready, 1)

            def aggregate_stats(b):
                for w in range(W):
                    nc.vector.bn_aggr(out=mean_var[:, b, w, :], in_=stats[:, w, :]).then_inc(stats_aggregated, 1)

            def add_eps(b):
                nc.vector.tensor_scalar(var_eps[:, b, :], mean_var[:, b, :, 1], EPS, None, ALU.add).then_inc(var_ready, 1)

            def group(g, b):
                turn_units(g, range(0, 4))
                copy_sums(g - 1, 1 - b)
                turn_units(g, range(4, 8))
                add_residual(g - 1, 1 - b)
                dve.wait_ge(h_ready, g)
                turn_units(g, range(8, 9))
                row_stats(1 - b)
                dve.wait_ge(stats_ready, g * W)
                turn_units(g, range(9, 10))
                aggregate_stats(1 - b)
                dve.wait_ge(stats_aggregated, g * W)
                turn_units(g, range(10, 11))
                add_eps(1 - b)
                turn_units(g, range(11, UNITS))

            dve.wait_ge(x_loaded, 2 * Q * 16)
            for c in range(C):
                steps = slice(c * J * D, (c + 1) * J * D)
                nc.vector.scalar_tensor_tensor(out=x_drop[:, steps], in0=x_drop[:, steps], scalar=P_DROP,
                                               in1=x_sb[:, steps], op0=ALU.is_ge, op1=ALU.mult).then_inc(x_dropped, 1)
            turn_units(0, range(UNITS), buffers_used=False)
            group(1, 1)
            with dve.Fori(1, G // 2) as pair:
                group(2 * pair, 0)
                group(2 * pair + 1, 1)
            copy_sums(G - 1, 1)
            add_residual(G - 1, 1)
            dve.wait_ge(h_ready, G)
            row_stats(1)
            dve.wait_ge(stats_ready, G * W)
            aggregate_stats(1)
            dve.wait_ge(stats_aggregated, G * W)
            add_eps(1)
            h_rows = h[:, 1, :].rearrange("p (w d) -> p w d", w=W)
            nc.vector.tensor_tensor(h_rows, h_rows, mean_var[:, 1, :, 0:1].broadcast_to([P, W, D]),
                                    ALU.subtract).then_inc(last_centred, 1)
            dve.wait_ge(out_stored, (G // 2 - 1) * Q * 16)
            dve.wait_ge(last_centred, 1)
            dve.wait_ge(rstd_ready, G)
            nc.vector.tensor_tensor(y[:, 1, :].rearrange("p (w d) -> p w d", w=W), h_rows,
                                    rstd[:, 1, :].rearrange("p (w d) -> p w d", d=1).broadcast_to([P, W, D]),
                                    ALU.mult).then_inc(last_y_ready, 1)

        @block.tensor
        def _(pe):
            def contract(g, b, chunks, first=False, bank_used=True):
                for c in chunks:
                    pe.wait_ge(unit_turned, g * UNITS + (c + 1) * Q)
                    if first:
                        pe.wait_ge(x_dropped, c + 1)
                    if c == 0 and bank_used:
                        pe.wait_ge(sums_copied, g - 1)
                    for j in range(J):
                        half = j % 2
                        i = c * J + j
                        last = nc.tensor.matmul(acc[b][half * D:(half + 1) * D, :], x_drop[:, i * D:(i + 1) * D],
                                                adj_t[:, c % 2, j * ROWS:(j + 1) * ROWS],
                                                start=(c == 0 and j < 2), stop=(c == C - 1 and j >= J - 2))
                    last.then_inc(chunk_used, 1)

            def contract_by_unit(g, b, c):
                for a in range(Q):
                    pe.wait_ge(unit_turned, g * UNITS + c * Q + a + 1)
                    for j in range(J):
                        half = j % 2
                        i = c * J + j
                        last = nc.tensor.matmul(acc[b][half * D:(half + 1) * D, a * RP:(a + 1) * RP],
                                                x_drop[:, i * D:(i + 1) * D],
                                                adj_t[:, c % 2, j * ROWS + a * RP:j * ROWS + (a + 1) * RP],
                                                start=False, stop=(c == C - 1 and a == Q - 1 and j >= J - 2))
                last.then_inc(chunk_used, 1)

            def fold_halves(g):
                pe.wait_ge(sums_copied, g + 1)
                for w in range(W):
                    last = nc.tensor.matmul(agg[:, w * D:(w + 1) * D], sums[:, w * P:(w + 1) * P], fold[:, :],
                                            start=True, stop=True)
                last.then_inc(agg_ready, 1)

            def group(g, b):
                contract(g, b, range(0, 1))
                fold_halves(g - 1)
                contract(g, b, range(1, C))

            contract(0, 0, range(C), first=True, bank_used=False)
            contract(1, 1, range(0, 1), bank_used=False)
            pe.wait_ge(const_ready, 1)
            fold_halves(0)
            contract(1, 1, range(1, C))
            with pe.Fori(1, G // 2 - 1) as pair:
                group(2 * pair, 0)
                group(2 * pair + 1, 1)
            group(G - 2, 0)
            contract(G - 1, 1, range(0, 1))
            fold_halves(G - 2)
            contract(G - 1, 1, range(1, C - 2))
            contract_by_unit(G - 1, 1, C - 2)
            contract_by_unit(G - 1, 1, C - 1)
            fold_halves(G - 1)

        @block.gpsimd
        def _(pool):
            def take_root(g, b):
                pool.wait_ge(var_ready, g + 1)
                nc.gpsimd.tensor_tensor(rstd[:, b, :], var_eps[:, b, :], neg_half[:, :], ALU.pow).then_inc(rstd_ready, 1)

            def normalise(g, b):
                take_root(g, b)
                h_rows = h[:, b, :].rearrange("p (w d) -> p w d", w=W)
                nc.gpsimd.tensor_tensor(h_rows, h_rows, mean_var[:, b, :, 0:1].broadcast_to([P, W, D]),
                                        ALU.subtract).then_inc(centred, 1)
                pool.wait_ge(rstd_ready, g + 1)
                pool.wait_ge(centred, g + 1)
                nc.gpsimd.tensor_tensor(y[:, b, :].rearrange("p (w d) -> p w d", w=W), h_rows,
                                        rstd[:, b, :].rearrange("p (w d) -> p w d", d=1).broadcast_to([P, W, D]),
                                        ALU.mult).then_inc(h_free, 1)

            def store(g, groups):
                pool.wait_ge(h_free, g + groups + 2)
                blocks = W // E
                for q in range(Q):
                    pool.dma_start(out_v[q, :, bass.ds(g * blocks, groups * blocks), :],
                                   y[q * B:(q + 1) * B, 0:groups, :].rearrange("p b (k f) -> p (b k) f", f=E * D)
                                   ).then_inc(out_stored, 16)

            pool.sem_inc(h_free, 2)
            nc.gpsimd.memset(fold[:, :], 0.0).then_inc(fold_step, 1)
            nc.gpsimd.memset(neg_half[:, :], -0.5).then_inc(fold_step, 1)
            pool.wait_ge(fold_step, 2)
            nc.gpsimd.affine_select(out=fold[:, :], in_=fold[:, :], compare_op=ALU.not_equal, fill=1.0, base=0,
                                    pattern=[[-1, D]], channel_multiplier=1).then_inc(fold_step, 1)
            pool.wait_ge(fold_step, 3)
            nc.gpsimd.affine_select(out=fold[:, :], in_=fold[:, :], compare_op=ALU.not_equal, fill=1.0, base=-D,
                                    pattern=[[-1, D]], channel_multiplier=1).then_inc(const_ready, 1)
            for b in range(2):
                normalise(b, b)
            store(0, 2)
            with pool.Fori(1, G // 2 - 1) as pair:
                pool.wait_ge(out_stored, pair * Q * 16)
                for b in range(2):
                    normalise(2 * pair + b, b)
                store(2 * pair, 2)
            pool.wait_ge(out_stored, (G // 2 - 1) * Q * 16)
            normalise(G - 2, 0)
            store(G - 2, 1)
            take_root(G - 1, 1)
            pool.wait_ge(out_stored, G // 2 * Q * 16)


def kernel(x, adj, L0_gnn_u):
    import numpy as np
    import concourse.bacc as bacc
    from concourse.bass_utils import run_bass_kernel_spmd

    nc = bacc.Bacc("TRN2", target_bir_lowering=False, num_devices=1)
    arrays, args = {}, []
    for name, a in (("x", x), ("adj", adj), ("u", L0_gnn_u)):
        a = np.ascontiguousarray(a)
        arrays[name] = a
        args.append(nc.dram_tensor(name, a.shape, mybir.dt.from_np(a.dtype), kind="ExternalInput").ap())
    out = nc.dram_tensor("out", x.shape, F32, kind="ExternalOutput").ap()
    build(nc, *args, out)
    r = run_bass_kernel_spmd(nc, [arrays], core_ids=[0])
    return r.results[0]["out"]
```
